# Optimizing a Trainium2 kernel written in Bass

```python
import numpy as np
import jax
import jax.numpy as jnp

def _softmax(x, axis=-1):
    return jax.nn.softmax(x, axis=axis)

def _gelu(x):
    return jax.nn.gelu(x, approximate=True)

def _silu(x):
    return jax.nn.silu(x)

def _sigmoid(x):
    return jax.nn.sigmoid(x)

def _layernorm(x, axis=-1, eps=1e-05):
    m = jnp.mean(x, axis=axis, keepdims=True)
    v = jnp.var(x, axis=axis, keepdims=True)
    return (x - m) / jnp.sqrt(v + eps)

def _scatter_add(tgt, idx, src, axis=0):
    return tgt.at[idx].add(src)

def _segment_sum(src, seg, n):
    return jax.ops.segment_sum(src, seg, n)
kernel_name = 'mk_gnn_resnorm_d1_gnn_r64_e632d4'

def setup_inputs(seed: int=0):
    np.random.seed(seed)
    _w = jnp.asarray

    def _rec_inputs():
        import jax
        import jax.numpy as jnp
        _gk = jax.random.key(seed)
        x = -0.000202 + 1 * jax.random.normal(jax.random.fold_in(_gk, 1), (100000, 64), jnp.float32)
        src = jax.random.randint(jax.random.fold_in(_gk, 2), (50000,), 0, 100000, jnp.int32)
        dst = jnp.minimum((100000 * jax.random.uniform(jax.random.fold_in(_gk, 3), (50000,)) ** 2.0).astype(jnp.int32), 99999)
        _o = jnp.argsort(dst, stable=True)
        src = src[_o]
        dst = dst[_o]
        edge_attr_32 = 0.000189758 + 1.00013 * jax.random.normal(jax.random.fold_in(_gk, 12), (50000, 32), jnp.float32)
        return (x, src, dst, edge_attr_32)
    x, src, dst, edge_attr_32 = _rec_inputs()

    def _L0_gnn_setup():
        import jax, jax.numpy as jnp
        import numpy as np
        N = 100000
        E = 25000
        ENC_EDGE = 32
        ENC_NODE = 64
        HIDDEN = 128
        key = jax.random.key(seed)
        ks = jax.random.split(key, 8)
        x = jax.random.normal(ks[0], (N, ENC_NODE), dtype=jnp.float32)
        edge_index = jax.random.randint(ks[1], (2, E), 0, N, dtype=jnp.int64)
        edge_attr = jax.random.normal(ks[2], (E, ENC_EDGE), dtype=jnp.float32)
        u = jax.random.normal(ks[3], (256, ENC_NODE), dtype=jnp.float32)
        batch = jax.random.randint(ks[4], (N,), 0, 256, dtype=jnp.int64)
        in1 = ENC_EDGE + ENC_NODE
        lim1 = float(np.sqrt(6.0 / (in1 + HIDDEN)))
        W1 = jax.random.uniform(ks[5], (in1, HIDDEN), minval=-lim1, maxval=lim1, dtype=jnp.float32)
        b1 = jnp.full((HIDDEN,), 0.01, dtype=jnp.float32)
        in2 = HIDDEN + ENC_NODE
        lim2 = float(np.sqrt(6.0 / (in2 + ENC_NODE)))
        W2 = jax.random.uniform(ks[6], (in2, ENC_NODE), minval=-lim2, maxval=lim2, dtype=jnp.float32)
        b2 = jnp.full((ENC_NODE,), 0.01, dtype=jnp.float32)
        return {'x': x, 'edge_index': edge_index, 'edge_attr': edge_attr, 'u': u, 'batch': batch, 'W1': W1, 'b1': b1, 'W2': W2, 'b2': b2}
    _L0_gnn_all = _L0_gnn_setup()
    _L0_gnn_in = {k: v for k, v in _L0_gnn_all.items() if k in ('u', 'W1', 'b1', 'W2', 'b2')}
    del _L0_gnn_all
    return {'x': x, 'src': src, 'dst': dst, 'edge_attr_32': edge_attr_32, 'L0_gnn_u': _L0_gnn_in['u'], 'L0_gnn_W1': _L0_gnn_in['W1'], 'L0_gnn_b1': _L0_gnn_in['b1'], 'L0_gnn_W2': _L0_gnn_in['W2'], 'L0_gnn_b2': _L0_gnn_in['b2']}

def reference(x, src, dst, edge_attr_32, L0_gnn_u, L0_gnn_W1, L0_gnn_b1, L0_gnn_W2, L0_gnn_b2):
    import jax
    import jax.numpy as jnp

    def _L0_gnn_ref(x, edge_index, edge_attr, u, batch, W1, b1, W2, b2):
        import jax, jax.numpy as jnp
        import numpy as np
        N = 100000
        E = 25000
        ENC_EDGE = 32
        ENC_NODE = 64
        HIDDEN = 128
        row, col = (edge_index[0], edge_index[1])
        msg = jnp.concatenate([x[row], edge_attr], axis=1)
        msg = msg @ W1 + b1
        agg = jax.ops.segment_sum(msg, col, num_segments=x.shape[0])
        out = jnp.concatenate([x, agg], axis=1)
        return out @ W2 + b2
    edge_index = jnp.stack([src, dst])
    batch0 = jnp.zeros((100000,), jnp.int32)
    x = _layernorm(x + _L0_gnn_ref(x, edge_index, edge_attr_32, L0_gnn_u, batch0, L0_gnn_W1, L0_gnn_b1, L0_gnn_W2, L0_gnn_b2), axis=-1)
    return x

_drawn_inputs = setup_inputs


def setup_inputs(seed=0):
    import zlib

    import numpy as np

    out = dict(_drawn_inputs(seed))
    spreads = {'L0_gnn_b1': (0.009999999776482582, 0.2), 'L0_gnn_b2': (0.009999999776482582, 0.2)}
    factors = {}
    for name, (base, spread) in spreads.items():
        noise = np.random.default_rng([zlib.crc32(name.encode()), seed]).standard_normal(out[name].shape)
        drawn = base * np.exp(spread * noise) if base else spread * noise
        out[name] = jnp.asarray(drawn.astype(out[name].dtype))
    for name, factor in factors.items():
        out[name] = (out[name] * factor).astype(out[name].dtype)
    return out
```

```python
import numpy as np
import concourse.bass as bass
from concourse import mybir
from contextlib import ExitStack

N, C = 100000, 64
E, CE = 50000, 32
H = 128
P = 128
F = C + CE + 1

CB = 4
BATCHES = 98
CHUNKS = BATCHES * CB
FULL_CHUNKS = E // P
LAST_CHUNK = -(-E // P) - 1
E_TAIL = E - FULL_CHUNKS * P

A = 2
GN = A * P
G = 4
BN = G * GN
BLOCKS = -(-N // BN)
PAIRS = BLOCKS // 2
FULL_BLOCKS = N // BN
N_TAIL = N - FULL_BLOCKS * BN
TAIL_GROUPS = N_TAIL // GN
TAIL_PARTS = (N_TAIL - TAIL_GROUPS * GN) // A
FAR = float(1 << 20)
EPS = 1e-5

assert BATCHES == BLOCKS == 2 * PAIRS and LAST_CHUNK < CHUNKS - 1 and BLOCKS <= P


def gnn_residual_layernorm(nc, x, src, dst, edge_attr, W1, b1, W2, b2, out, scratch):
    f32, bf16, i32 = mybir.dt.float32, mybir.dt.bfloat16, mybir.dt.int32
    ALU, ACT, AX = mybir.AluOpType, mybir.ActivationFunctionType, mybir.AxisListType

    ctx = ExitStack()
    with ctx:
        def sb(name, shape, dt=f32):
            return ctx.enter_context(nc.sbuf_tensor(name, shape, dt))

        def ps(name, shape):
            return ctx.enter_context(nc.psum_tensor(name, shape, f32))

        def sem(name):
            return ctx.enter_context(nc.semaphore(name))

        def sem2(name):
            return [sem(f"{name}{h}") for h in range(2)]

        ident = sb("ident", [P, P])
        ones = sb("ones", [P, P])
        ones_bf = sb("ones_bf", [65, P], bf16)
        node_of_col = sb("node_of_col", [P, A, P])
        group_base = sb("group_base", [P, BLOCKS * G])
        block_base = sb("block_base", [P, G])
        chunk_up = sb("chunk_up", [P, CHUNKS])
        chunk_down = sb("chunk_down", [P, CHUNKS])
        eps = sb("eps", [P, 1])
        w1aug = sb("w1aug", [CE + C + 1, H])
        w1aug_t = sb("w1aug_t", [H, F])
        w2_agg = sb("w2_agg", [H, C])
        wz = sb("wz", [F, C])
        wx = sb("wx", [P, P])
        wsum = sb("wsum", [P, 4])
        b2c = sb("b2c", [65, C])
        b2r = sb("b2r", [65, C])
        b2part = sb("b2part", [65, 3, C], bf16)
        b2rows = sb("b2rows", [65, G * A, C], bf16)
        src_ck = sb("src_ck", [P, 4, P], i32)
        dst_ck = sb("dst_ck", [P, 4, P], i32)
        src_ckf = sb("src_ckf", [P, 4, P])
        dst_ckf = sb("dst_ckf", [P, 4, P])
        dst_far = sb("dst_far", [P, 4, P])
        least = sb("least", [P, 4])
        most = sb("most", [P, 4])
        diag = sb("diag", [P, 4, P])
        least_row = sb("least_row", [P, CHUNKS])
        most_row = sb("most_row", [P, CHUNKS])
        src_idx = sb("src_idx", [P, CHUNKS], i32)
        dst_of = sb("dst_of", [P, CHUNKS])
        block_end = sb("block_end", [P, G])
        below = sb("below", [P, CHUNKS])
        holds = sb("holds", [P, CHUNKS])
        score = sb("score", [P, CHUNKS])
        far_first = sb("far_first", [P, G])
        last = sb("last", [P, G])
        first = sb("first", [P, G])
        extra = sb("extra", [P, G])
        steps = sb("steps", [P, 2 * G], i32)
        steps_row = sb("steps_row", [1, BLOCKS * 2 * G], i32)
        src_now = [sb(f"src_now{h}", [P, CB], i32) for h in range(2)]
        feat = [sb(f"feat{h}", [P, CB, F]) for h in range(2)]
        feat_t = [sb(f"feat_t{h}", [F, CB * P]) for h in range(2)]
        z = sb("z", [P, CHUNKS, C])
        xin = [sb(f"xin{h}", [P, G, A * C]) for h in range(2)]
        x_t = [sb(f"x_t{h}", [P, G * P]) for h in range(2)]
        onehot = [sb(f"onehot{h}", [P, G, 2, A, P]) for h in range(2)]
        onehot_x = [sb(f"onehot_x{h}", [P, A, P]) for h in range(2)]
        square = [sb(f"square{h}", [P, G * A, C]) for h in range(2)]
        sumsq = [sb(f"sumsq{h}", [P, G * A]) for h in range(2)]
        std = [sb(f"std{h}", [P, G * A]) for h in range(2)]
        rstd = [sb(f"rstd{h}", [P, G * A]) for h in range(2)]
        yout = [sb(f"yout{h}", [P, G * A, C]) for h in range(2)]

        ps_t = [ps(f"ps_t{h}", [P, 512]) for h in range(2)]
        ps_z = [ps(f"ps_z{h}", [P, 512]) for h in range(2)]
        ps_y = [ps(f"ps_y{h}", [P, 512]) for h in range(2)]
        ps_a = ps("ps_a", [P, 512])
        ps_b = ps("ps_b", [P, 512])

        s_const = sem("consts_made")
        s_clear = sem("buffers_cleared")
        s_ident = sem("ident_step")
        s_wload = sem("weights_loaded")
        s_iload = sem("indices_loaded")
        s_w = sem("weight_step_pe")
        s_dve = sem("dve_step")
        s_ckf = sem("indices_as_float")
        s_idx_t = sem("indices_transposed")
        s_idx = sem("index_tables_ready")
        s_diag = sem("diag_ready")
        s_rows = sem("bound_rows_done")
        s_bound = sem("bounds_ready")
        s_steps = sem("steps_ready")
        s_stored_steps = sem("steps_stored")
        s_loaded_steps = sem("steps_loaded")
        s_wready = sem("weights_ready")
        s_now = sem("src_staged")
        s_go = sem("gathers_go")
        gathered = sem2("gathered")
        ea_loaded = sem2("edge_attr_loaded")
        feat_used = sem2("feat_transposed")
        feat_ready = sem2("feat_t_ready")
        z_done = sem2("z_in_psum")
        z_kept = sem2("z_kept")
        x_loaded = sem2("x_loaded")
        x_used = sem2("x_transposed")
        x_ready = sem2("x_t_ready")
        hot_ready = sem("onehot_ready")
        hotx_ready = sem2("onehot_x_ready")
        hotx_used = sem2("onehot_x_used")
        y_done = sem2("y_in_psum")
        squared = sem2("squared")
        summed = sem2("summed")
        rooted = sem2("rooted")
        s_dve2 = sem2("rstd_ready")
        out_ready = sem2("out_ready")
        out_stored = sem2("out_stored")

        x_blocks = x[0:FULL_BLOCKS * BN, :].rearrange("(b g p a) c -> b p g (a c)", g=G, p=P, a=A)
        out_blocks = out[0:FULL_BLOCKS * BN, :].rearrange("(b g p a) c -> b p g (a c)", g=G, p=P, a=A)
        ea_batches = edge_attr[0:FULL_CHUNKS // CB * CB * P, :].rearrange("(b k p) c -> b p k c", k=CB, p=P)

        def tail_parts(t):
            whole = t[FULL_BLOCKS * BN:FULL_BLOCKS * BN + TAIL_GROUPS * GN, :]
            return (whole.rearrange("(g p a) c -> p g (a c)", g=TAIL_GROUPS, p=P),
                    t[FULL_BLOCKS * BN + TAIL_GROUPS * GN:N, :].rearrange("(p a) c -> p (a c)", a=A))

        def wait_rounds(eng, semaphore, k, per_round=1):
            if not (isinstance(k, int) and k == 0):
                eng.wait_ge(semaphore, per_round * k)

        block = ctx.enter_context(nc.Block())

        @block.sync
        def _(sp):
            sp.wait_ge(s_clear, 6)
            for ck, ap in ((src_ck, src), (dst_ck, dst)):
                rows = FULL_CHUNKS - 3 * P
                sp.dma_start(ck[:, 0:3, :], ap[0:3 * P * P].rearrange("(t p f) -> p t f", t=3, p=P)).then_inc(s_iload, 16)
                sp.dma_start(ck[0:rows, 3, :], ap[3 * P * P:FULL_CHUNKS * P].rearrange("(p f) -> p f", p=rows)).then_inc(s_iload, 16)
                sp.dma_start(ck[rows:rows + 1, 3, 0:E_TAIL], ap[FULL_CHUNKS * P:E].rearrange("(o f) -> o f", o=1)).then_inc(s_iload, 16)
            sp.dma_start(w1aug[0:C + CE, :], W1[:, :]).then_inc(s_wload, 16)
            sp.dma_start(w1aug[C + CE:F, :], b1.rearrange("(o f) -> o f", o=1)).then_inc(s_wload, 16)
            sp.dma_start(w2_agg[:, :], W2[C:C + H, :]).then_inc(s_wload, 16)
            for r in range(A):
                sp.dma_start(wx[r * C:(r + 1) * C, r * C:(r + 1) * C], W2[0:C, :]).then_inc(s_wload, 16)
            for r in range(3):
                sp.dma_start(b2c[32 * r:32 * r + 1, :], b2.rearrange("(o f) -> o f", o=1)).then_inc(s_wload, 16)
            for h in range(2):
                sp.dma_start(xin[h][:, :, :], x_blocks[h]).then_inc(x_loaded[h], 16)

            def load_ea(k, h, src_ap):
                wait_rounds(sp, feat_used[h], k)
                sp.dma_start(feat[h][:, :, C:C + CE], src_ap).then_inc(ea_loaded[h], 16)

            for h in range(2):
                load_ea(0, h, ea_batches[h])
            with sp.Fori(1, PAIRS - 1) as k:
                for h in range(2):
                    load_ea(k, h, ea_batches[2 * k + h])
            load_ea(PAIRS - 1, 0, ea_batches[BATCHES - 2])
            sp.wait_ge(feat_used[1], PAIRS - 1)
            e0 = (BATCHES - 1) * CB * P
            tail_chunks = FULL_CHUNKS - (BATCHES - 1) * CB
            sp.dma_start(feat[1][:, 0:tail_chunks, C:C + CE],
                         edge_attr[e0:FULL_CHUNKS * P, :].rearrange("(k p) c -> p k c", p=P)).then_inc(ea_loaded[1], 16)
            sp.dma_start(feat[1][0:E_TAIL, tail_chunks, C:C + CE], edge_attr[FULL_CHUNKS * P:E, :]).then_inc(ea_loaded[1], 16)

            sp.wait_ge(s_steps, 1)
            sp.dma_start(scratch.rearrange("(b k) -> b k", b=BLOCKS), steps[0:BLOCKS, :]).then_inc(s_stored_steps, 16)
            sp.wait_ge(s_stored_steps, 16)
            sp.dma_start(steps_row[:, :], scratch.rearrange("(o n) -> o n", o=1)).then_inc(s_loaded_steps, 16)

            def load_x(k, h, src_ap):
                wait_rounds(sp, x_used[h], k)
                sp.dma_start(xin[h][:, :, :], src_ap).then_inc(x_loaded[h], 16)

            def store(k, h, dst_ap):
                sp.wait_ge(out_ready[h], k + 1)
                sp.dma_start(dst_ap, yout[h][:, :, :].rearrange("p (g a) c -> p g (a c)", g=G)).then_inc(out_stored[h], 16)

            with sp.Fori(0, PAIRS - 2) as k:
                for h in range(2):
                    load_x(k + 1, h, x_blocks[2 * k + 2 + h])
                    store(k, h, out_blocks[2 * k + h])
            load_x(PAIRS - 1, 0, x_blocks[BLOCKS - 2])
            store(PAIRS - 2, 0, out_blocks[BLOCKS - 4])
            sp.wait_ge(x_used[1], PAIRS - 1)
            whole, cut = tail_parts(x)
            sp.dma_start(xin[1][:, 0:TAIL_GROUPS, :], whole).then_inc(x_loaded[1], 16)
            sp.dma_start(xin[1][0:TAIL_PARTS, TAIL_GROUPS, :], cut).then_inc(x_loaded[1], 16)
            store(PAIRS - 2, 1, out_blocks[BLOCKS - 3])
            store(PAIRS - 1, 0, out_blocks[BLOCKS - 2])
            sp.wait_ge(out_ready[1], PAIRS)
            whole, cut = tail_parts(out)
            yt = yout[1][:, :, :].rearrange("p (g a) c -> p g (a c)", g=G)
            sp.dma_start(whole, yt[:, 0:TAIL_GROUPS, :]).then_inc(out_stored[1], 16)
            sp.dma_start(cut, yt[0:TAIL_PARTS, TAIL_GROUPS, :]).then_inc(out_stored[1], 16)
            sp.wait_ge(out_stored[0], 16 * PAIRS)
            sp.wait_ge(out_stored[1], 16 * (PAIRS + 1))

        @block.gpsimd
        def _(pool):
            nc.gpsimd.memset(src_ck[:, :, :], 0).then_inc(s_clear, 1)
            nc.gpsimd.memset(dst_ck[:, :, :], -1).then_inc(s_clear, 1)
            nc.gpsimd.memset(wx[:, :], 0.0).then_inc(s_clear, 1)
            nc.gpsimd.memset(b2c[:, :], 0.0).then_inc(s_clear, 1)
            for h in range(2):
                nc.gpsimd.memset(feat[h][:, :, :], 1.0).then_inc(s_clear, 1)
            nc.gpsimd.memset(ident[:, :], 0.0).then_inc(s_ident, 1)
            pool.wait_ge(s_ident, 1)
            nc.gpsimd.affine_select(out=ident[:, :], in_=ident[:, :], compare_op=ALU.not_equal, fill=1.0,
                                    base=0, pattern=[[-1, P]], channel_multiplier=1).then_inc(s_const, 1)
            nc.gpsimd.memset(ones[:, :], 1.0).then_inc(s_const, 1)
            nc.gpsimd.memset(ones_bf[:, :], 1.0).then_inc(s_const, 1)
            nc.gpsimd.memset(b2rows[:, :, :], 0.0).then_inc(s_const, 1)
            nc.gpsimd.memset(eps[:, :], EPS).then_inc(s_const, 1)
            nc.gpsimd.iota(node_of_col[:, :, :], pattern=[[1, A], [A, P]], base=0, channel_multiplier=0,
                           allow_small_or_imprecise_dtypes=True).then_inc(s_const, 1)
            nc.gpsimd.iota(group_base[:, :], pattern=[[GN, BLOCKS * G]], base=0, channel_multiplier=0,
                           allow_small_or_imprecise_dtypes=True).then_inc(s_const, 1)
            nc.gpsimd.iota(block_base[:, :], pattern=[[GN, G]], base=0, channel_multiplier=BN,
                           allow_small_or_imprecise_dtypes=True).then_inc(s_const, 1)
            nc.gpsimd.iota(chunk_up[:, :], pattern=[[1, CHUNKS]], base=1, channel_multiplier=0,
                           allow_small_or_imprecise_dtypes=True).then_inc(s_const, 1)
            nc.gpsimd.iota(chunk_down[:, :], pattern=[[-1, CHUNKS]], base=512, channel_multiplier=0,
                           allow_small_or_imprecise_dtypes=True).then_inc(s_const, 1)

            pool.wait_ge(s_idx, 1)
            def gather(k, h):
                wait_rounds(pool, gathered[h], k, 16 * CB)
                nc.gpsimd.tensor_copy(src_now[h][:, :], src_idx[:, bass.ds(2 * CB * k + CB * h, CB)]).then_inc(s_now, 1)
                pool.wait_ge(s_now, 2 * k + h + 1)
                wait_rounds(pool, feat_used[h], k)
                pool.sem_inc(s_go)
                for c in range(CB):
                    nc.gpsimd.indirect_dma_start(
                        out=feat[h][:, c, 0:C], out_offset=None, in_=x[:, :],
                        in_offset=bass.IndirectOffsetOnAxis(ap=src_now[h][:, c:c + 1], axis=0)).then_inc(gathered[h], 16)

            for h in range(2):
                gather(0, h)
            with pool.Fori(1, PAIRS) as k:
                for h in range(2):
                    gather(k, h)

        @block.tensor
        def _(pe):
            pe.wait_ge(s_wload, 16 * 8)
            pe.wait_ge(s_const, 10)
            nc.tensor.transpose(ps_a[0:H, 0:F], w1aug[:, :], ident[0:F, 0:F]).then_inc(s_w, 1)
            pe.wait_ge(s_ckf, 2)
            for t in range(4):
                nc.tensor.transpose(ps_t[0][:, t * P:(t + 1) * P], src_ckf[:, t, :], ident[:, :])
            for t in range(4):
                tr = nc.tensor.transpose(ps_t[1][:, t * P:(t + 1) * P], dst_ckf[:, t, :], ident[:, :])
            tr.then_inc(s_idx_t, 1)
            pe.wait_ge(s_wready, 1)
            nc.tensor.matmul(ps_z[0][0:F, 0:C], w1aug_t[:, :], w2_agg[:, :], start=True, stop=True).then_inc(s_w, 1)
            for n, bank in ((1, ps_a), (2, ps_b)):
                pe.wait_ge(s_diag, n)
                for t in range(4):
                    mm = nc.tensor.matmul(bank[:, t * P:(t + 1) * P], ones[:, :], diag[:, t, :], start=True, stop=True)
                mm.then_inc(s_rows, 1)

            pe.wait_ge(s_wready, 2)
            pe.wait_ge(s_idx, 1)

            def turn(k, h, loads=1):
                pe.wait_ge(gathered[h], 16 * CB * (k + 1))
                pe.wait_ge(ea_loaded[h], 16 * (k + loads))
                wait_rounds(pe, feat_ready[h], k)
                for c in range(CB):
                    tr = nc.tensor.transpose(ps_t[h][0:F, c * P:(c + 1) * P], feat[h][:, c, :], ident[:, :])
                tr.then_inc(feat_used[h], 1)

            def message(k, h):
                pe.wait_ge(feat_ready[h], k + 1)
                wait_rounds(pe, z_kept[h], k)
                for c in range(CB):
                    mm = nc.tensor.matmul(ps_z[h][:, c * C:(c + 1) * C], feat_t[h][:, c * P:(c + 1) * P], wz[:, :],
                                          start=True, stop=True)
                mm.then_inc(z_done[h], 1)

            def edge_round(k):
                turn(k, 1)
                message(k, 0)
                turn(k + 1, 0)
                message(k, 1)

            turn(0, 0)
            edge_round(0)
            with pe.Fori(1, PAIRS - 1) as k:
                edge_round(k)
            turn(PAIRS - 1, 1, loads=2)
            message(PAIRS - 1, 0)
            message(PAIRS - 1, 1)
            for h in range(2):
                pe.wait_ge(z_kept[h], PAIRS)
                pe.wait_ge(feat_ready[h], PAIRS)

            pe.wait_ge(s_loaded_steps, 16)
            for s in range(2):
                pe.sem_inc(hotx_used[s])
            pairs_done = pe.alloc_register("pairs_done_pe")
            nc.tensor.reg_mov(pairs_done, 0)

            def turn_x(k, h, loads=1):
                pe.wait_ge(x_loaded[h], 16 * (k + loads))
                wait_rounds(pe, x_ready[h], k)
                for g in range(G):
                    tr = nc.tensor.transpose(ps_t[h][:, g * P:(g + 1) * P], xin[h][:, g, :], ident[:, :])
                tr.then_inc(x_used[h], 1)

            def block_sum(k, h):
                b = 2 * k + h
                row = steps_row[0:1, bass.ds(b * 2 * G, G)]
                _, firsts = nc.values_load_multi_w_load_instructions(
                    row, engines=[mybir.EngineType.PE], min_val=0, max_val=LAST_CHUNK, skip_runtime_bounds_check_because="the table is made within these bounds")
                row = steps_row[0:1, bass.ds(b * 2 * G + G, G)]
                _, pairs = nc.values_load_multi_w_load_instructions(
                    row, engines=[mybir.EngineType.PE], min_val=0, max_val=CHUNKS // 2, skip_runtime_bounds_check_because="the table is made within these bounds")
                wait_rounds(pe, out_ready[h], k)
                nc.tensor.matmul(ps_y[h][:, :], ones_bf[:, :], b2rows[:, :, :].rearrange("p n c -> p (n c)"),
                                 start=True, stop=False)
                for g in range(G):
                    pe.wait_ge(hot_ready, G * b + g + 1)
                    for s in range(2):
                        for a in range(A):
                            col = (g * A + a) * C
                            nc.tensor.matmul(ps_y[h][:, col:col + C], onehot[h][:, g, s, a, :], z[:, firsts[g] + s, :],
                                             start=False, stop=False)
                    with pe.If(pairs[g] > 0):
                        with pe.Fori(0, pairs[g]) as n:
                            nc.tensor.reg_add(pairs_done, pairs_done, 1)
                            done = pe.snap(pairs_done)
                            chunk = nc.s_assert_within(pe.snap(firsts[g] + 2 * n), 0, CHUNKS - 4, skip_runtime_bounds_check_because="the table of steps ends every range before the last chunk")
                            for s in range(2):
                                pe.wait_ge(hotx_ready[s], done)
                                for a in range(A):
                                    col = (g * A + a) * C
                                    mm = nc.tensor.matmul(ps_y[h][:, col:col + C], onehot_x[s][:, a, :],
                                                          z[:, chunk + (2 + s), :], start=False, stop=False)
                                mm.then_inc(hotx_used[s], 1)
                pe.wait_ge(x_ready[h], k + 1)
                for g in range(G):
                    mm = nc.tensor.matmul(ps_y[h][:, g * A * C:(g + 1) * A * C], x_t[h][:, g * P:(g + 1) * P], wx[:, :],
                                          start=False, stop=(g == G - 1))
                mm.then_inc(y_done[h], 1)

            def node_round(k):
                turn_x(k, 1)
                block_sum(k, 0)
                turn_x(k + 1, 0)
                block_sum(k, 1)

            turn_x(0, 0)
            node_round(0)
            with pe.Fori(1, PAIRS - 1) as k:
                node_round(k)
            turn_x(PAIRS - 1, 1, loads=2)
            block_sum(PAIRS - 1, 0)
            block_sum(PAIRS - 1, 1)

        @block.scalar
        def _(act):
            def keep_feat(k, h):
                act.wait_ge(feat_used[h], k + 1)
                wait_rounds(act, z_done[h], k)
                nc.scalar.activation(feat_t[h][:, :], ps_t[h][0:F, :], ACT.Copy).then_inc(feat_ready[h], 1)

            for h in range(2):
                keep_feat(0, h)
            with act.Fori(1, PAIRS) as k:
                for h in range(2):
                    keep_feat(k, h)

            def keep_x(k, h):
                act.wait_ge(x_used[h], k + 1)
                wait_rounds(act, y_done[h], k)
                nc.scalar.activation(x_t[h][:, :], ps_t[h][:, :], ACT.Copy).then_inc(x_ready[h], 1)

            def squares(k, h):
                act.wait_ge(y_done[h], k + 1)
                wait_rounds(act, summed[h], k)
                nc.scalar.activation(square[h][:, :, :], ps_y[h][:, :].rearrange("p (n c) -> p n c", c=C),
                                     ACT.Square).then_inc(squared[h], 1)
                act.wait_ge(summed[h], k + 1)
                wait_rounds(act, out_ready[h], k)
                nc.scalar.activation(std[h][:, :], sumsq[h][:, :], ACT.Sqrt, bias=eps[:, :], scale=1.0 / C).then_inc(rooted[h], 1)

            def node_round(k):
                keep_x(k, 1)
                squares(k, 0)
                keep_x(k + 1, 0)
                squares(k, 1)

            keep_x(0, 0)
            node_round(0)
            with act.Fori(1, PAIRS - 1) as k:
                node_round(k)
            keep_x(PAIRS - 1, 1)
            squares(PAIRS - 1, 0)
            squares(PAIRS - 1, 1)

        @block.vector
        def _(dve):
            done = [0]

            def link(ins):
                done[0] += 1
                ins.then_inc(s_dve, 1)
                dve.wait_ge(s_dve, done[0])

            dve.wait_ge(s_iload, 16 * 6)
            nc.vector.tensor_copy(src_ckf[:, :, :], src_ck[:, :, :]).then_inc(s_ckf, 1)
            nc.vector.tensor_copy(dst_ckf[:, :, :], dst_ck[:, :, :]).then_inc(s_ckf, 1)
            dve.wait_ge(s_idx_t, 1)
            nc.vector.tensor_copy(dst_of[:, :], ps_t[1][:, 0:CHUNKS]).then_inc(s_dve, 1)
            nc.vector.tensor_copy(src_idx[:, :], ps_t[0][:, 0:CHUNKS]).then_inc(s_idx, 1)
            done[0] += 1
            dve.wait_ge(s_w, 1)
            nc.vector.tensor_copy(w1aug_t[:, :], ps_a[0:H, 0:F]).then_inc(s_wready, 1)
            dve.wait_ge(s_w, 2)
            dve.wait_ge(s_const, 10)
            link(nc.vector.tensor_copy(wz[:, :], ps_z[0][0:F, 0:C]))
            link(nc.vector.tensor_tensor(wx[:, :], wx[:, :], ident[:, :], ALU.add))
            link(nc.vector.reduce_sum(wsum[0:F, 0:1], wz[:, :], axis=AX.X))
            link(nc.vector.reduce_sum(wsum[:, 1:2], wx[:, :], axis=AX.X))
            link(nc.vector.reduce_sum(wsum[0:65, 2:3], b2c[:, :], axis=AX.X))
            link(nc.vector.tensor_scalar(wsum[:, 3:4], wsum[:, 1:2], 1.0 / C, None, ALU.mult))
            link(nc.vector.tensor_scalar(wsum[0:F, 0:1], wsum[0:F, 0:1], 1.0 / C, None, ALU.mult))
            link(nc.vector.tensor_scalar(wsum[0:65, 2:3], wsum[0:65, 2:3], 1.0 / C, None, ALU.mult))
            link(nc.vector.tensor_scalar(wz[:, :], wz[:, :], wsum[0:F, 0:1], None, ALU.subtract))
            for r in range(A):
                part = slice(r * C, (r + 1) * C)
                link(nc.vector.tensor_scalar(wx[part, part], wx[part, part], wsum[part, 3:4], None, ALU.subtract))
            link(nc.vector.tensor_scalar(b2c[:, :], b2c[:, :], wsum[0:65, 2:3], None, ALU.subtract))
            for n in range(3):
                link(nc.vector.tensor_copy(b2part[:, n, :], b2c[:, :]))
                if n < 2:
                    link(nc.vector.tensor_tensor(b2r[:, :], b2c[:, :], b2part[:, n, :], ALU.subtract))
                    link(nc.vector.tensor_copy(b2c[:, :], b2r[:, :]))
            for n in range(3):
                for q in range(G * A):
                    ins = nc.vector.tensor_copy(b2rows[32 * n:32 * n + 1, q, :], b2part[32 * n:32 * n + 1, n, :])
            ins.then_inc(s_wready, 1)

            link(nc.vector.reduce_max(most[:, :], dst_ckf[:, :, :], axis=AX.X))
            link(nc.vector.tensor_scalar(dst_far[:, :, :], dst_ckf[:, :, :], 0.0, FAR, ALU.is_lt, ALU.mult))
            link(nc.vector.tensor_tensor(dst_far[:, :, :], dst_far[:, :, :], dst_ckf[:, :, :], ALU.add))
            link(nc.vector.tensor_reduce(least[:, :], dst_far[:, :, :], AX.X, ALU.min))
            for n, (bound, bank, row) in enumerate(((least, ps_a, least_row), (most, ps_b, most_row))):
                for t in range(4):
                    ins = nc.vector.tensor_scalar(diag[:, t, :], ident[:, :], bound[:, t:t + 1], None, ALU.mult)
                ins.then_inc(s_diag, 1)
                dve.wait_ge(s_rows, n + 1)
                link(nc.vector.tensor_copy(row[:, :], bank[:, 0:CHUNKS]))
            link(nc.vector.tensor_scalar(block_end[:, :], block_base[:, :], float(GN - 1), None, ALU.add))
            for g in range(G):
                link(nc.vector.tensor_scalar(below[:, :], least_row[:, :], block_end[:, g:g + 1], None, ALU.is_le))
                link(nc.vector.scalar_tensor_tensor(out=holds[:, :], in0=most_row[:, :], scalar=block_base[:, g:g + 1],
                                                    in1=below[:, :], op0=ALU.is_ge, op1=ALU.mult))
                link(nc.vector.tensor_tensor(score[:, :], holds[:, :], chunk_down[:, :], ALU.mult))
                link(nc.vector.reduce_max(far_first[:, g:g + 1], score[:, :], axis=AX.X))
                link(nc.vector.tensor_tensor(score[:, :], holds[:, :], chunk_up[:, :], ALU.mult))
                link(nc.vector.reduce_max(last[:, g:g + 1], score[:, :], axis=AX.X))
            link(nc.vector.tensor_scalar(first[:, :], far_first[:, :], -1.0, 512.0, ALU.mult, ALU.add))
            link(nc.vector.tensor_scalar(first[:, :], first[:, :], float(LAST_CHUNK), None, ALU.min))
            link(nc.vector.tensor_copy(steps[:, 0:G], first[:, :]))
            link(nc.vector.tensor_tensor(extra[:, :], last[:, :], first[:, :], ALU.subtract))
            link(nc.vector.tensor_scalar(extra[:, :], extra[:, :], -1.0, 0.0, ALU.add, ALU.max))
            link(nc.vector.tensor_copy(steps[:, G:2 * G], extra[:, :]))
            nc.vector.tensor_scalar(steps[:, G:2 * G], steps[:, G:2 * G], 1, None, ALU.arith_shift_right).then_inc(s_steps, 1)

            with dve.Fori(0, PAIRS) as k:
                for h in range(2):
                    dve.wait_ge(z_done[h], k + 1)
                    nc.vector.tensor_copy(z[:, bass.ds(2 * CB * k + CB * h, CB), :],
                                          ps_z[h][:, 0:CB * C].rearrange("p (k c) -> p k c", c=C)).then_inc(z_kept[h], 1)

            dve.wait_ge(s_loaded_steps, 16)
            pairs_done = dve.alloc_register("pairs_done_dve")
            nc.vector.reg_mov(pairs_done, 0)

            def one_hots(k, h):
                b = 2 * k + h
                row = steps_row[0:1, bass.ds(b * 2 * G, G)]
                _, firsts = nc.values_load_multi_w_load_instructions(
                    row, engines=[mybir.EngineType.DVE], min_val=0, max_val=LAST_CHUNK, skip_runtime_bounds_check_because="the table is made within these bounds")
                row = steps_row[0:1, bass.ds(b * 2 * G + G, G)]
                _, pairs = nc.values_load_multi_w_load_instructions(
                    row, engines=[mybir.EngineType.DVE], min_val=0, max_val=CHUNKS // 2, skip_runtime_bounds_check_because="the table is made within these bounds")
                wait_rounds(dve, y_done[h], k)
                for g in range(G):
                    base = group_base[:, bass.ds(b * G + g, 1)]
                    for s in range(2):
                        ins = nc.vector.tensor_scalar(onehot[h][:, g, s, :, :], node_of_col[:, :, :], base,
                                                      dst_of[:, bass.ds(firsts[g] + s, 1)], ALU.add, ALU.is_equal)
                    ins.then_inc(hot_ready, 1)
                    with dve.If(pairs[g] > 0):
                        with dve.Fori(0, pairs[g]) as n:
                            nc.vector.reg_add(pairs_done, pairs_done, 1)
                            turn_no = dve.snap(pairs_done)
                            chunk = nc.s_assert_within(dve.snap(firsts[g] + 2 * n), 0, CHUNKS - 4, skip_runtime_bounds_check_because="the table of steps ends every range before the last chunk")
                            for s in range(2):
                                dve.wait_ge(hotx_used[s], turn_no)
                                nc.vector.tensor_scalar(onehot_x[s][:, :, :], node_of_col[:, :, :], base,
                                                        dst_of[:, bass.ds(chunk + (2 + s), 1)],
                                                        ALU.add, ALU.is_equal).then_inc(hotx_ready[s], 1)

            def add_up(k, h):
                dve.wait_ge(squared[h], k + 1)
                wait_rounds(dve, rooted[h], k)
                nc.vector.reduce_sum(sumsq[h][:, :], square[h][:, :, :], axis=AX.X).then_inc(summed[h], 1)

            def normalize(k, h):
                dve.wait_ge(rooted[h], k + 1)
                nc.vector.reciprocal(rstd[h][:, :], std[h][:, :]).then_inc(s_dve2[h], 1)
                dve.wait_ge(s_dve2[h], k + 1)
                wait_rounds(dve, out_stored[h], k, 16)
                nc.vector.tensor_tensor(yout[h][:, :, :], ps_y[h][:, :].rearrange("p (n c) -> p n c", c=C),
                                        rstd[h][:, :].rearrange("p (n o) -> p n o", o=1).to_broadcast([P, G * A, C]),
                                        ALU.mult).then_inc(out_ready[h], 1)

            def node_round(k):
                one_hots(k, 1)
                add_up(k, 0)
                normalize(k, 0)
                one_hots(k + 1, 0)
                add_up(k, 1)
                normalize(k, 1)

            one_hots(0, 0)
            node_round(0)
            with dve.Fori(1, PAIRS - 1) as k:
                node_round(k)
            one_hots(PAIRS - 1, 1)
            for h in range(2):
                add_up(PAIRS - 1, h)
                normalize(PAIRS - 1, h)


def kernel(x, src, dst, edge_attr_32, L0_gnn_u, L0_gnn_W1, L0_gnn_b1, L0_gnn_W2, L0_gnn_b2):
    import concourse.bacc as bacc
    from concourse.bass_utils import run_bass_kernel_spmd

    nc = bacc.Bacc("TRN2", target_bir_lowering=False, num_devices=1)
    given = {"x": x, "src": src, "dst": dst, "edge_attr": edge_attr_32,
             "W1": L0_gnn_W1, "b1": L0_gnn_b1, "W2": L0_gnn_W2, "b2": L0_gnn_b2}
    arrays, aps = {}, []
    for name, value in given.items():
        a = np.ascontiguousarray(value)
        arrays[f"in_{name}"] = a
        aps.append(nc.dram_tensor(f"in_{name}", a.shape, mybir.dt.from_np(a.dtype), kind="ExternalInput").ap())
    out = nc.dram_tensor("out_0", (N, C), mybir.dt.float32, kind="ExternalOutput").ap()
    scratch = nc.dram_tensor("steps_scratch", (BLOCKS * 2 * G,), mybir.dt.int32, kind="Internal").ap()
    gnn_residual_layernorm(nc, *aps, out, scratch)
    result = run_bass_kernel_spmd(nc, [arrays], core_ids=[0])
    return result.results[0]["out_0"]
```
